# Optimizing a Trainium2 kernel written in Bass

```python
import numpy as np
import jax
import jax.numpy as jnp

def _softmax(x, axis=-1):
    return jax.nn.softmax(x, axis=axis)

def _gelu(x):
    return jax.nn.gelu(x, approximate=True)

def _silu(x):
    return jax.nn.silu(x)

def _sigmoid(x):
    return jax.nn.sigmoid(x)

def _layernorm(x, axis=-1, eps=1e-05):
    m = jnp.mean(x, axis=axis, keepdims=True)
    v = jnp.var(x, axis=axis, keepdims=True)
    return (x - m) / jnp.sqrt(v + eps)

def _scatter_add(tgt, idx, src, axis=0):
    return tgt.at[idx].add(src)

def _segment_sum(src, seg, n):
    return jax.ops.segment_sum(src, seg, n)
kernel_name = 'mk_gnn_resnorm_d2_gnn_r8_62692c'

def setup_inputs(seed: int=0):
    np.random.seed(seed)
    _w = jnp.asarray

    def _rec_inputs():
        import jax
        import jax.numpy as jnp
        _gk = jax.random.key(seed)
        x = -0.000202 + 1 * jax.random.normal(jax.random.fold_in(_gk, 1), (6250, 128), jnp.float32)
        src = jax.random.randint(jax.random.fold_in(_gk, 2), (100000,), 0, 6250, jnp.int32)
        dst = jax.random.randint(jax.random.fold_in(_gk, 3), (100000,), 0, 6250, jnp.int32)
        _o = jnp.argsort(dst, stable=True)
        src = src[_o]
        dst = dst[_o]
        edge_attr_64 = -0.000128692 + 0.999872 * jax.random.normal(jax.random.fold_in(_gk, 11), (100000, 64), jnp.float32)
        return (x, src, dst, edge_attr_64)
    x, src, dst, edge_attr_64 = _rec_inputs()

    def _L0_gnn_setup():
        import jax, jax.numpy as jnp
        import numpy as np
        N_NODES = 6250
        NUM_HYPEREDGES = 6250
        key = jax.random.key(seed)
        k1, k2, k3, k4, k5 = jax.random.split(key, 5)
        E = 200000
        F_IN, F_OUT = (128, 128)
        X = jax.random.normal(k1, (N_NODES, F_IN), dtype=jnp.float32)
        nodes = jax.random.randint(k2, (E,), 0, N_NODES, dtype=jnp.int64)
        hedges = jax.random.randint(k3, (E,), 0, NUM_HYPEREDGES, dtype=jnp.int64)
        edge_index = jnp.stack([nodes, hedges], axis=0)
        W = jax.random.normal(k4, (F_IN, F_OUT), dtype=jnp.float32) * (1.0 / np.sqrt(F_IN))
        b = jax.random.normal(k5, (F_OUT,), dtype=jnp.float32) * 0.02
        return {'X': X, 'edge_index': edge_index, 'W': W, 'b': b}
    _L0_gnn_all = _L0_gnn_setup()
    _L0_gnn_in = {k: v for k, v in _L0_gnn_all.items() if k in ('W', 'b')}
    del _L0_gnn_all

    def _L1_gnn_setup():
        import jax, jax.numpy as jnp
        import numpy as np
        N_NODES = 5000
        N_EDGES = 80000
        NODE_DIM = 128
        EDGE_DIM = 64
        HIDDEN_DIM = 256
        LN_EPS = 1e-05
        key = jax.random.key(seed)
        ks = jax.random.split(key, 10)
        x = jax.random.normal(ks[0], (N_NODES, NODE_DIM), dtype=jnp.float32)
        edge_attr = jax.random.normal(ks[1], (N_EDGES, EDGE_DIM), dtype=jnp.float32)
        edge_index = jax.random.randint(ks[2], (2, N_EDGES), 0, N_NODES, dtype=jnp.int64)
        in_dim = NODE_DIM + EDGE_DIM
        W1 = jax.random.normal(ks[3], (in_dim, HIDDEN_DIM), dtype=jnp.float32) / np.sqrt(in_dim)
        b1 = jnp.zeros((HIDDEN_DIM,), dtype=jnp.float32)
        W2 = jax.random.normal(ks[4], (HIDDEN_DIM, NODE_DIM), dtype=jnp.float32) / np.sqrt(HIDDEN_DIM)
        b2 = jnp.zeros((NODE_DIM,), dtype=jnp.float32)
        gamma = jnp.ones((NODE_DIM,), dtype=jnp.float32)
        beta = jnp.zeros((NODE_DIM,), dtype=jnp.float32)
        Wu = jax.random.normal(ks[5], (NODE_DIM, NODE_DIM), dtype=jnp.float32) / np.sqrt(NODE_DIM)
        bu = jnp.zeros((NODE_DIM,), dtype=jnp.float32)
        return {'x': x, 'edge_attr': edge_attr, 'edge_index': edge_index, 'W1': W1, 'b1': b1, 'W2': W2, 'b2': b2, 'gamma': gamma, 'beta': beta, 'Wu': Wu, 'bu': bu}
    _L1_gnn_all = _L1_gnn_setup()
    _L1_gnn_in = {k: v for k, v in _L1_gnn_all.items() if k in ('W1', 'b1', 'W2', 'b2', 'gamma', 'beta', 'Wu', 'bu')}
    del _L1_gnn_all
    return {'x': x, 'src': src, 'dst': dst, 'edge_attr_64': edge_attr_64, 'L0_gnn_W': _L0_gnn_in['W'], 'L0_gnn_b': _L0_gnn_in['b'], 'L1_gnn_W1': _L1_gnn_in['W1'], 'L1_gnn_b1': _L1_gnn_in['b1'], 'L1_gnn_W2': _L1_gnn_in['W2'], 'L1_gnn_b2': _L1_gnn_in['b2'], 'L1_gnn_gamma': _L1_gnn_in['gamma'], 'L1_gnn_beta': _L1_gnn_in['beta'], 'L1_gnn_Wu': _L1_gnn_in['Wu'], 'L1_gnn_bu': _L1_gnn_in['bu']}

def reference(x, src, dst, edge_attr_64, L0_gnn_W, L0_gnn_b, L1_gnn_W1, L1_gnn_b1, L1_gnn_W2, L1_gnn_b2, L1_gnn_gamma, L1_gnn_beta, L1_gnn_Wu, L1_gnn_bu):
    import jax
    import jax.numpy as jnp

    def _L0_gnn_ref(X, edge_index, W, b):
        import jax, jax.numpy as jnp
        import numpy as np
        N_NODES = 6250
        NUM_HYPEREDGES = 6250
        nodes = edge_index[0]
        hedges = edge_index[1]
        ones = jnp.ones(nodes.shape[0], dtype=X.dtype)
        x = X @ W
        deg_e = jax.ops.segment_sum(ones, hedges, num_segments=NUM_HYPEREDGES)
        B_inv = jnp.where(deg_e > 0, 1.0 / deg_e, 0.0)
        deg_v = jax.ops.segment_sum(ones, nodes, num_segments=N_NODES)
        D_inv = jnp.where(deg_v > 0, 1.0 / deg_v, 0.0)
        m = jax.ops.segment_sum(x[nodes], hedges, num_segments=NUM_HYPEREDGES)
        m = m * B_inv[:, None]
        out = jax.ops.segment_sum(m[hedges], nodes, num_segments=N_NODES)
        out = out * D_inv[:, None] + b
        return jax.nn.softmax(out, axis=1)

    def _L1_gnn_ref(x, edge_attr, edge_index, W1, b1, W2, b2, gamma, beta, Wu, bu):
        import jax, jax.numpy as jnp
        import numpy as np
        N_NODES = 5000
        N_EDGES = 80000
        NODE_DIM = 128
        EDGE_DIM = 64
        HIDDEN_DIM = 256
        LN_EPS = 1e-05
        src = edge_index[0]
        dst = edge_index[1]
        m_in = jnp.concatenate([x[src], edge_attr], axis=-1)
        h = jax.nn.relu(m_in @ W1 + b1)
        m = jax.nn.relu(h @ W2 + b2)
        agg = jax.ops.segment_sum(m, dst, num_segments=x.shape[0])
        out = x + agg
        mu = jnp.mean(out, axis=-1, keepdims=True)
        var = jnp.mean(jnp.square(out - mu), axis=-1, keepdims=True)
        normed = (out - mu) * jax.lax.rsqrt(var + LN_EPS) * gamma + beta
        return jax.nn.relu(normed) @ Wu + bu
    edge_index = jnp.stack([src, dst])
    x = _layernorm(x + _L0_gnn_ref(x, edge_index, L0_gnn_W, L0_gnn_b), axis=-1)
    x = _layernorm(x + _L1_gnn_ref(x, edge_attr_64, edge_index, L1_gnn_W1, L1_gnn_b1, L1_gnn_W2, L1_gnn_b2, L1_gnn_gamma, L1_gnn_beta, L1_gnn_Wu, L1_gnn_bu), axis=-1)
    return x

_drawn_inputs = setup_inputs


def setup_inputs(seed=0):
    import zlib

    import numpy as np

    out = dict(_drawn_inputs(seed))
    spreads = {'L1_gnn_b1': (0.0, 0.1),
     'L1_gnn_b2': (0.0, 0.1),
     'L1_gnn_gamma': (1.0, 0.2),
     'L1_gnn_beta': (0.0, 0.1),
     'L1_gnn_bu': (0.0, 0.1)}
    factors = {'L0_gnn_W': 64.0, 'L0_gnn_b': 64.0}
    for name, (base, spread) in spreads.items():
        noise = np.random.default_rng([zlib.crc32(name.encode()), seed]).standard_normal(out[name].shape)
        drawn = base * np.exp(spread * noise) if base else spread * noise
        out[name] = jnp.asarray(drawn.astype(out[name].dtype))
    for name, factor in factors.items():
        out[name] = (out[name] * factor).astype(out[name].dtype)
    return out
```

```python
from contextlib import ExitStack

import concourse.bass as bass
from concourse import mybir

F32 = mybir.dt.float32
BF16 = mybir.dt.bfloat16
I32 = mybir.dt.int32
U32 = mybir.dt.uint32
ALU = mybir.AluOpType
ACT = mybir.ActivationFunctionType
AX = mybir.AxisListType

P = 128
NODES = 6250
EDGES = 100000
D = 128
DE = 64
DH = 256
K = 4
GE = K * P
RING = 4
TURNS = 4
NG = -(-EDGES // GE)
IT = NG // RING
EPAD = NG * GE
T = -(-NODES // P)
NPAD = T * P
W = 64
NWIDE = (T + 1) * P
TS = 7
STEPS = T // TS
DX = D + 1
NB = 10
MT = (T + 1) // NB
LN_EPS = 1e-5
IN_RANGE = "indices are below the number of nodes"
LOADS_W = 12
assert IT * RING == NG and STEPS * TS == T and NB * MT == T + 1 and NG % 2 == 0


def build(nc, x, src_cols, src_all, dst_all, dst_groups, src_row, edge_t, W0, b0, W1, b1, W2, b2, gamma, beta, Wu, bu, out):
    with ExitStack() as ctx:
        def sb(name, shape, dt=F32):
            return scopes[-1].enter_context(nc.sbuf_tensor(name, shape, dt))

        scopes = [ctx]

        def phase(name, former=None):
            while former is not None and scopes[-1] is not former:
                scopes.pop().close()
            if former is not None:
                scopes.pop().close()
            scopes.append(ctx.enter_context(ExitStack()))
            return scopes[-1]

        def sem(name):
            return ctx.enter_context(nc.semaphore(name))

        def sems(name, n=RING):
            return [sem(f"{name}{i}") for i in range(n)]

        meta_d = nc.dram_tensor("meta_d", (NG,), I32, kind="Internal").ap()
        lo_d = nc.dram_tensor("lo_d", (NG,), F32, kind="Internal").ap()
        m_d = nc.dram_tensor("m_d", (NWIDE, DX), F32, kind="Internal").ap()
        tables_d = [nc.dram_tensor(f"table{k}_d", (NWIDE, DX), F32, kind="Internal").ap() for k in range(K)]
        p_d = nc.dram_tensor("p_d", (NPAD, DH), F32, kind="Internal").ap()

        ident = sb("ident", [P, P])
        earlier = sb("earlier", [P, P], BF16)
        iota_i = sb("iota_i", [P, W], I32)
        iota = sb("iota", [P, W])
        spare_i = sb("spare_i", [P, 1], I32)
        win_start_i = sb("win_start_i", [P, P], I32)
        spare = sb("spare", [P, 1])
        ones = sb("ones", [P, P])
        ones_b = sb("ones_b", [P, P], BF16)
        zeros_b = sb("zeros_b", [P, GE], BF16)
        eps = sb("eps", [P, 1])
        W0_sb = sb("W0_sb", [D, D])
        W1a_sb = sb("W1a_sb", [D, DH])
        W1b_sb = sb("W1b_sb", [2 * DE, DH])
        W2_sb = sb("W2_sb", [P, 2, D])
        Wu_sb = sb("Wu_sb", [D, D])
        b0_sb = sb("b0_sb", [P, D])
        gamma_sb = sb("gamma_sb", [D, 1])
        beta_sb = sb("beta_sb", [D, 1])
        b2_sb = sb("b2_sb", [P, D])
        bias = sb("bias", [3, D + DH])
        bias_b = sb("bias_b", [3, D + DH], BF16)
        bias3 = sb("bias3", [3, D + DH], BF16)
        bias3_k = sb("bias3_k", [3, K, D], BF16)

        lohi = sb("lohi", [NG // 2, 2, 2])
        span_i = sb("span_i", [NG // 2, 2], I32)
        wins = sb("wins", [NG // 2, 2])
        meta_i = sb("meta_i", [NG // 2, 2], I32)
        meta = sb("meta", [1, NG], I32)
        lo_bc = sb("lo_bc", [P, NG])
        rel = sb("rel", [P, NG, K])
        src_f = sb("src_f", [P, NG, K])

        acc = sb("acc", [P, 2, NWIDE])
        x_sb = sb("x_sb", [P, T, D])
        x1 = x_sb

        ix = [sb(f"ix{j}", [P, K], I32) for j in range(RING)]
        rows = [sb(f"rows{j}", [P, K, DH]) for j in range(RING)]
        rows_a = [r[:, 0:K // 2, :].rearrange("p k (a f) -> p (k a) f", a=2) for r in rows]
        win_start = sb("win_start", [P, P])
        hot_b = [sb(f"hot_b{j}", [P, K, W], BF16) for j in range(RING)]
        hot_xb = sb("hot_xb", [P, K, W], BF16)
        hot_x = sb("hot_x", [P, K, W])
        rel_x = sb("rel_x", [P, K])
        dup = sb("dup", [P, K])
        spare_if = sb("spare_if", [P, K])
        to = [sb(f"to{j}", [P, K], U32) for j in range(RING)]
        m_win = [sb(f"m_win{j}", [W, DX]) for j in range(RING)]
        m_win_x = sb("m_win_x", [W, DX])

        inv = [sb(f"inv{h}", [P, TS]) for h in range(2)]
        negmax = [sb(f"negmax{h}", [P, TS]) for h in range(2)]
        esum = [sb(f"esum{h}", [P, TS]) for h in range(2)]
        stats = sb("stats", [P, TS, 6])
        mv, std, rstd, shift = ([sb(f"{n}{h}", [P, TS, c][:2 + (c > 1)]) for h in range(2)]
                                for n, c in (("mv", 2), ("std", 1), ("rstd", 1), ("shift", 1)))
        mv2, std2, rstd2, shift2 = ([sb(f"{n}2_{h}", [P, TS, c][:2 + (c > 1)]) for h in range(2)]
                                    for n, c in (("mv", 2), ("std", 1), ("rstd", 1), ("shift", 1)))
        ps = ctx.enter_context(nc.psum_tensor("ps", [P, 8, 512], F32))

        def banks(a, n=1):
            return ps[:, a:a + n, :].rearrange("p b c -> p (b c)")

        early = phase("early")
        zero_rows = sb("zero_rows", [P, 10 * DX])
        dst_g = sb("dst_g", [NG // 2, 2, GE], I32)
        dst_i = sb("dst_i", [P, NG, K], I32)
        src_i = sb("src_i", [P, NG, K], I32)
        hot = [sb(f"hot{j}", [P, K, W]) for j in range(RING)]
        src_b = [sb(f"src_b{j}", [P, K, P], I32) for j in range(RING)]
        same = [sb(f"same{j}", [P, K, P], BF16) for j in range(RING)]
        same_before = sb("same_before", [P, K, P], BF16)
        mix = [sb(f"mix{j}", [W, K, P]) for j in range(RING)]
        mix_x = sb("mix_x", [W, K, P])
        sums = [sb(f"sums{j}", [P, K, DX]) for j in range(RING)]
        m_sb = sb("m_sb", [P, T + 1, DX])
        sum_t = [sb(f"sum_t{h}", [P, MT, P]) for h in range(2)]
        inv_deg = sb("inv_deg", [P, T + 1])

        phase("late", early)
        sm = [sb(f"sm{h}", [P, TS, D]) for h in range(2)]
        row_t = [sb(f"row_t{h}", [P, TS * P]) for h in range(2)]
        row = [sb(f"row{h}", [P, TS, D]) for h in range(2)]
        agg_t = [sb(f"agg_t{h}", [P, TS, P]) for h in range(2)]
        inner = phase("x")
        tab = [sb(f"tab{h}", [P, K, TS * DX]) for h in range(2)]
        p_sb = [sb(f"p_sb{h}", [P, TS, DH]) for h in range(2)]
        y = [sb(f"y{h}", [P, TS, D]) for h in range(2)]
        phase("c", inner)
        ea = [sb(f"ea{j}", [2 * DE, GE // 2]) for j in range(RING)]
        hid = [sb(f"hid{j}", [P, 2, GE]) for j in range(2)]
        pre = [sb(f"pre{j}", [P, K, DH]) for j in range(2)]
        msg = [sb(f"msg{j}", [P, 3, K, D], BF16) for j in range(2)]
        rest = [sb(f"rest{j}", [P, K, D]) for j in range(2)]

        pool_const = sem("pool_const")
        pool_turn = sem("pool_turn")
        cst = sem("cst")
        ld_dst_g, ld_dst, ld_src, ld_w, ld_x = sem("ld_dst_g"), sem("ld_dst"), sem("ld_src"), sem("ld_w"), sem("ld_x")
        meta_made, meta_out, meta_in = sem("meta_made"), sem("meta_out"), sem("meta_in")
        counts_zero, zero_made, tables_zero = sem("counts_zero"), sem("zero_made"), sem("tables_zero")

        ix_in, a_got = sems("ix_in"), sems("a_got")
        a_hot, a_sum, a_added = sem("a_hot"), sem("a_sum"), sem("a_added")
        ax_hot, ax_sum = sem("ax_hot"), sem("ax_sum")
        m_counts, m_picked, m_mul, m_made = (sem(s) for s in ("m_counts", "m_picked", "m_mul", "m_made"))
        acc_zero = sem("acc_zero")
        m_out = sems("m_out", 2)

        b_src_in, b_win_in = sems("b_src_in"), sems("b_win_in")
        b_same, b_to, b_mix, b_mixed, b_sum, b_sums = (sem(s) for s in ("b_same", "b_to", "b_mix", "b_mixed", "b_sum", "b_sums"))
        b_put = [sems(f"b_put{j}_", K) for j in range(RING)]
        bx_hot, bx_win, bx_mix, bx_mixed, bx_sum = (sem(s) for s in ("bx_hot", "bx_win", "bx_mix", "bx_mixed", "bx_sum"))

        t_in = sems("t_in", 2)
        t_half, t_logits, t_exp, t_inv, t_prob, t_y = (
            sem(s) for s in ("t_half", "t_logits", "t_exp", "t_inv", "t_prob", "t_y"))
        v_var, v_std, v_shift = (sem(s) for s in ("v_var", "v_std", "v_shift"))
        n_x1, n_t, n_tc, n_p, n_pc = (sem(s) for s in ("n_x1", "n_t", "n_tc", "n_p", "n_pc"))
        x1_kept = sems("x1_kept", 2)
        p_out = sems("p_out", 2)

        cx_in, ea_in, c_got = sems("cx_in"), sems("ea_in"), sems("c_got")
        c_edge, c_pre, c_t, c_hid, c_m, c_part, c_rest, c_part2, c_msg, c_hot, c_sum, c_added = (
            sem(s) for s in ("c_edge", "c_pre", "c_t", "c_hid", "c_m", "c_part", "c_rest", "c_part2", "c_msg", "c_hot",
                             "c_sum", "c_added"))
        c_open, c_b2 = sem("c_open"), sem("c_b2")
        cx_hot, cx_sum = sem("cx_hot"), sem("cx_sum")

        f_agg, f_res, f_var, f_std, f_shift, f_nrm, f_t, f_z, f_lin = (
            sem(s) for s in ("f_agg", "f_res", "f_var", "f_std", "f_shift", "f_nrm", "f_t", "f_z", "f_lin"))
        f_var2, f_std2, f_shift2, f_o = (sem(s) for s in ("f_var2", "f_std2", "f_shift2", "f_o"))
        f_out = sems("f_out", 2)

        def group_meta(eng, g):
            v = eng.value_load(meta[0:1, bass.ds(g, 1)], min_val=0, max_val=NODES * P + P - 1)
            return v >> 7, v & (P - 1)

        def further_windows(eng, count, wins, body):
            with eng.If(wins > 1):
                with eng.Fori(1, wins) as w:
                    w = nc.s_assert_within(w, 1, (NODES - 1) // W + 1, skip_runtime_bounds_check_because=IN_RANGE)
                    body(w, eng.snap(count))
                    eng.reg_add(count, count, 1)

        def window_at(lo, w):
            return nc.s_assert_within(lo + w * W, 0, NODES, skip_runtime_bounds_check_because=IN_RANGE)

        def counter(eng, name):
            reg = eng.alloc_register(name)
            eng.reg_mov(reg, 0)
            return reg

        def after(n):
            return n + (1 + RING)

        def credit(eng, *signals):
            for s in signals:
                eng.sem_inc(s, RING)

        def stage_order(eng, lag, stages, steps=NG, ring=RING, turns=TURNS):
            def tick(n, i, c):
                for d, stage in stages:
                    if i is not None or 0 <= c - d < steps:
                        stage(n - d, (c - d) % ring, (c - d) // ring + (0 if i is None else i * turns))
            body = ring * turns
            loops = (steps - lag) // body
            for c in range(lag):
                tick(c, None, c)
            with eng.Fori(0, loops) as i:
                for u in range(body):
                    tick(i * body + (lag + u), i, lag + u)
            for c in range(lag + loops * body, steps + lag):
                tick(c, None, c)

        def groups(eng, body):
            stage_order(eng, 0, ((0, body),))

        def node_steps(eng, lag, *stages):
            stage_order(eng, lag, stages, STEPS, 2, 1)

        block = ctx.enter_context(nc.Block())

        @block.sync
        def _(sp):
            def indices_a(g, j, it):
                sp.wait_ge(a_got[j], it * (16 * K))
                sp.dma_start(ix[j][:, :], src_cols[bass.ds(g, 1), :, :].rearrange("o p k -> (o p) k")).then_inc(ix_in[j], 16)
            groups(sp, indices_a)

            sp.wait_ge(a_added, after(NG - 1))
            sp.dma_start(inv_deg[:, :], acc[0:1, 1, :].rearrange("o (p t) -> o p t", p=P)).then_inc(m_counts, 16)

            def m_rows(n, h, i):
                sp.wait_ge(m_made, after(n))
                sp.dma_start(m_d.rearrange("(p t) f -> p (t f)", p=P)[:, bass.ds(n * (MT * DX), MT * DX)],
                             m_sb[:, bass.ds(n * MT, MT), :].rearrange("p t f -> p (t f)")).then_inc(m_out[h], 16)
            stage_order(sp, 0, ((0, m_rows),), NB, 2, 1)

            sp.wait_ge(meta_in, 32)
            count = counter(sp, "bx_sp")

            def loads_b(g, j, it):
                lo, wins = group_meta(sp, g)
                sp.wait_ge(b_same, after(g - RING))
                sp.dma_start(src_b[j][:, :, :], src_row[bass.ds(g, 1), :].to_broadcast([P, GE])
                             .rearrange("p (k e) -> p k e", k=K)).then_inc(b_src_in[j], 16)
                sp.wait_ge(b_sum, after(g - RING))
                for h in range(2):
                    sp.wait_ge(m_out[h], 16 * (NB // 2))
                sp.dma_start(m_win[j][:, :], m_d[bass.ds(lo, W), :]).then_inc(b_win_in[j], 16)

                def further(w, n):
                    sp.wait_ge(bx_sum, n)
                    sp.dma_start(m_win_x[:, :], m_d[bass.ds(window_at(lo, w), W), :]).then_inc(bx_win, 16)
                further_windows(sp, count, wins, further)
            groups(sp, loads_b)

            for j in range(RING):
                for k in range(K):
                    sp.wait_ge(b_put[j][k], 16 * IT)

            def table_rows(s, h, i):
                sp.wait_ge(t_logits, after(s - 2))
                for k in range(K):
                    view = tables_d[k][0:NPAD, :].rearrange("(p t) f -> p (t f)", p=P)
                    sp.dma_start(tab[h][:, k, :], view[:, bass.ds(s * (TS * DX), TS * DX)]).then_inc(t_in[h], 16)

            def keep_x1(s, h, i):
                sp.wait_ge(n_x1, after(s))
                sp.dma_start(x_sb[:, bass.ds(s * TS, TS), :].rearrange("p t f -> p (t f)"),
                             row[h][:, :, :].rearrange("p t f -> p (t f)")).then_inc(x1_kept[h], 16)

            def p_rows(s, h, i):
                sp.wait_ge(n_pc, after(s))
                view = p_d.rearrange("(p t) f -> p (t f)", p=P)
                sp.dma_start(view[:, bass.ds(s * (TS * DH), TS * DH)],
                             p_sb[h][:, :, :].rearrange("p t f -> p (t f)")).then_inc(p_out[h], 16)
            node_steps(sp, 4, (0, table_rows), (3, keep_x1), (4, p_rows))

            def loads_c(g, j, it):
                sp.wait_ge(c_got[j], it * (16 * K))
                sp.dma_start(ix[j][:, :], src_cols[bass.ds(g, 1), :, :].rearrange("o p k -> (o p) k")).then_inc(cx_in[j], 16)
                sp.wait_ge(c_edge, after(g - RING))
                sp.dma_start(ea[j][:, :], edge_t[:, bass.ds(g * (GE // 2), GE // 2)]).then_inc(ea_in[j], 16)
            groups(sp, loads_c)

            def result_rows(s, h, i):
                sp.wait_ge(f_o, after(s))
                view = out.rearrange("(p t) f -> p (t f)", p=P)
                sp.dma_start(view[:, bass.ds(s * (TS * D), TS * D)],
                             sm[h][:, :, :].rearrange("p t f -> p (t f)")).then_inc(f_out[h], 16)
            node_steps(sp, 0, (0, result_rows))
            for h in range(2):
                sp.wait_ge(f_out[h], 16 * ((STEPS + 1 - h) // 2))

        @block.gpsimd
        def _(pool):
            credit(pool, t_half, t_prob, t_y, f_agg)
            pool.memset(ones[:, :], 1.0)
            pool.memset(ones_b[:, :], 1.0)
            pool.memset(zeros_b[:, :], 0.0)
            pool.memset(eps[:, :], LN_EPS)
            pool.memset(ident[:, :], 0.0)
            pool.memset(earlier[:, :], 1.0)
            pool.iota(iota_i[:, :], pattern=[[1, W]], base=0, channel_multiplier=0)
            pool.iota(win_start_i[:, :], pattern=[[W, P]], base=0, channel_multiplier=0)
            pool.iota(spare_i[:, :], pattern=[[1, 1]], base=NPAD, channel_multiplier=1).then_inc(pool_const, 1)
            pool.wait_ge(pool_const, 1)
            pool.affine_select(out=ident[:, :], in_=ident[:, :], compare_op=ALU.not_equal, fill=1.0,
                               base=0, pattern=[[-1, P]], channel_multiplier=1)
            pool.affine_select(out=earlier[:, :], in_=earlier[:, :], compare_op=ALU.is_gt, fill=0.0,
                               base=0, pattern=[[-1, P]], channel_multiplier=1)
            pool.memset(m_sb[:, :, D:DX], 1.0).then_inc(cst, 1)

            def gather_a(g, j, it):
                pool.wait_ge(ix_in[j], it * 16 + 16)
                pool.wait_ge(a_sum, after(g - RING))
                pool.sem_inc(pool_turn, 1)
                for k in range(K):
                    pool.indirect_dma_start(rows_a[j][:, k, :], None, x,
                                            bass.IndirectOffsetOnAxis(ix[j][:, k:k + 1].bitcast(U32), 0))\
                        .then_inc(a_got[j], 16)
            groups(pool, gather_a)

            pool.wait_ge(m_picked, after(NB - 1))
            pool.memset(acc[:, 0, :], 0.0).then_inc(acc_zero, 1)

            pool.wait_ge(tables_zero, 16 * 5 * K)

            def scatter_b(g, j, it):
                pool.wait_ge(b_to, after(g))
                pool.wait_ge(b_sums, after(g))
                for k in range(K):
                    pool.wait_ge(b_put[j - 1][k], it * 16 + (16 if j else 0))
                    pool.sem_inc(pool_turn, 1)
                    pool.indirect_dma_start(tables_d[k], bass.IndirectOffsetOnAxis(to[j][:, k:k + 1], 0),
                                            sums[j][:, k, :], None, bounds_check=NWIDE - 1, oob_is_err=True,
                                            compute_op=ALU.add).then_inc(b_put[j][k], 16)
            groups(pool, scatter_b)

            def add_pairs(s, h, i):
                pool.wait_ge(t_in[h], i * (16 * K) + 16 * K)
                for k in range(0, K, 2):
                    last = pool.tensor_tensor(tab[h][:, k, :], tab[h][:, k, :], tab[h][:, k + 1, :], ALU.add)
                last.then_inc(t_half, 1)

            def residual(s, h, i):
                pool.wait_ge(t_inv, after(s))
                pool.tensor_tensor(sm[h][:, :, :], sm[h][:, :, :], esum[h][:, :].unsqueeze(2).to_broadcast([P, TS, D]), ALU.mult)\
                    .then_inc(t_prob, 1)
                pool.wait_ge(t_prob, after(s))
                pool.wait_ge(n_x1, after(s - 2))
                pool.tensor_tensor(y[h][:, :, :], sm[h][:, :, :], x_sb[:, bass.ds(s * TS, TS), :], ALU.add).then_inc(t_y, 1)
            pool.wait_ge(ld_x, 16)
            node_steps(pool, 2, (2, residual), (0, add_pairs))

            for h in range(2):
                pool.wait_ge(p_out[h], 16 * ((STEPS + 1 - h) // 2))

            def gather_c(g, j, it):
                pool.wait_ge(cx_in[j], it * 16 + 16)
                pool.wait_ge(c_pre, after(g - RING))
                pool.sem_inc(pool_turn, 1)
                for k in range(K):
                    pool.indirect_dma_start(rows[j][:, k, :], None, p_d,
                                            bass.IndirectOffsetOnAxis(ix[j][:, k:k + 1].bitcast(U32), 0))\
                        .then_inc(c_got[j], 16)
            groups(pool, gather_c)

            pool.wait_ge(c_added, after(NG - 1))

            def pick_nodes(s, h, i):
                pool.wait_ge(f_res, after(s - 2))
                pool.tensor_copy(agg_t[h][:, :, :], acc[:, 0, 0:NPAD].rearrange("f (p t) -> f t p", t=T)
                                 [:, bass.ds(s * TS, TS), :]).then_inc(f_agg, 1)
            node_steps(pool, 0, (0, pick_nodes))

        @block.scalar
        def _(act):
            credit(act, m_picked, b_mixed, b_sums, t_exp, v_std, n_x1, n_pc, c_hid, c_part, c_part2,
                   c_b2, f_std, f_nrm, f_z, f_std2, f_o)
            act.dma_start(dst_g[:, :, :], dst_groups).then_inc(ld_dst_g, 16)
            act.dma_start(dst_i[:, :, :], dst_all).then_inc(ld_dst, 16)
            act.dma_start(src_i[:, :, :], src_all).then_inc(ld_src, 16)
            act.wait_ge(cst, 1)
            act.activation(acc[:, 1, :].rearrange("p (a n) -> p a n", n=P),
                           zeros_b[:, 0:P].unsqueeze(1).to_broadcast([P, NWIDE // P, P]), ACT.Copy).then_inc(counts_zero, 1)
            act.wait_ge(meta_made, 2)
            act.dma_start(meta_d.rearrange("(p a) -> p a", a=2), meta_i[:, :]).then_inc(meta_out, 16)
            act.dma_start(lo_d.rearrange("(p a) -> p a", a=2), lohi[:, 0, :]).then_inc(meta_out, 16)
            act.wait_ge(meta_out, 32)
            act.dma_start(meta[0:1, :], meta_d.rearrange("(a g) -> a g", a=1)).then_inc(meta_in, 16)
            act.dma_start(lo_bc[:, :], lo_d.rearrange("(a g) -> a g", a=1).to_broadcast([P, NG])).then_inc(meta_in, 16)
            for dst_ap, src_ap in ((W0_sb[:, :], W0), (W1a_sb[:, :], W1[0:D, :]), (W1b_sb[0:DE, :], W1[D:D + DE, :]),
                                   (W1b_sb[DE:, :], W1[D:D + DE, :]),
                                   (W2_sb[:, :, :], W2.rearrange("(c p) f -> p c f", p=P)), (Wu_sb[:, :], Wu),
                                   (b0_sb[:, :], b0.rearrange("(a f) -> a f", a=1).to_broadcast([P, D])),
                                   (b2_sb[:, :], b2.rearrange("(a f) -> a f", a=1).to_broadcast([P, D])),
                                   (bias[:, 0:D], bu.rearrange("(a f) -> a f", a=1).to_broadcast([3, D])),
                                   (bias[:, D:], b1.rearrange("(a f) -> a f", a=1).to_broadcast([3, DH]))):
                act.dma_start(dst_ap, src_ap).then_inc(ld_w, 16)
            with nc.allow_non_contiguous_dma(reason="scale and bias columns, loaded once"):
                act.dma_start(gamma_sb[:, :], gamma.rearrange("(p a) -> p a", a=1)).then_inc(ld_w, 16)
                act.dma_start(beta_sb[:, :], beta.rearrange("(p a) -> p a", a=1)).then_inc(ld_w, 16)
            act.activation(zero_rows[:, :].rearrange("p (a f) -> p a f", f=DX),
                           zeros_b[:, 0:DX].unsqueeze(1).to_broadcast([P, 10, DX]), ACT.Copy).then_inc(zero_made, 1)
            act.wait_ge(zero_made, 1)
            for k in range(K):
                view = tables_d[k].rearrange("(p r) f -> p (r f)", p=P)
                for c in range(5):
                    act.wait_ge(a_sum, after(9 * (5 * k + c)))
                    act.dma_start(view[:, c * 10 * DX:(c + 1) * 10 * DX], zero_rows[:, :]).then_inc(tables_zero, 16)
            act.wait_ge(a_sum, after(9 * 5 * K))
            act.dma_start(x_sb[:, :, :], x.rearrange("(p t) f -> p t f", p=P)).then_inc(ld_x, 16)

            act.wait_ge(a_added, after(NG - 1))

            def pick_m(n, h, i):
                act.wait_ge(m_mul, after(n - 2))
                act.activation(sum_t[h][:, :, :], acc[:, 0, :].rearrange("f (p t) -> f t p", t=T + 1)
                               [:, bass.ds(n * MT, MT), :], ACT.Copy).then_inc(m_picked, 1)
            stage_order(act, 0, ((0, pick_m),), NB, 2, 1)

            act.wait_ge(meta_in, 32)
            count = counter(act, "bx_act")

            def copies_b(g, j, it):
                lo, wins = group_meta(act, g)
                act.wait_ge(b_mix, after(g))
                act.activation(mix[j][:, :, :], ps[0:W, j % 2, :].rearrange("p (k e) -> p k e", k=K), ACT.Copy)\
                   .then_inc(b_mixed, 1)

                def further(w, n):
                    act.wait_ge(bx_mix, n + 1)
                    act.activation(mix_x[:, :, :], ps[0:W, 6, :].rearrange("p (k e) -> p k e", k=K), ACT.Copy)\
                       .then_inc(bx_mixed, 1)
                further_windows(act, count, wins, further)
                act.wait_ge(b_sum, after(g))
                for k in range(K):
                    act.wait_ge(b_put[j][k], it * 16)
                act.activation(sums[j][:, :, :].rearrange("p (b k) f -> p b (k f)", b=2),
                               ps[:, 2 + 2 * (j % 2):4 + 2 * (j % 2), 0:2 * DX], ACT.Copy).then_inc(b_sums, 1)
            groups(act, copies_b)

            def normed(s, h, i):
                act.wait_ge(n_t, after(s - 2))
                act.wait_ge(x1_kept[h], i * 16)
                act.wait_ge(v_shift, after(s))
                for u in range(TS):
                    last = act.activation(row[h][:, u, :], y[h][:, u, :], ACT.Identity, bias=shift[h][:, u:u + 1],
                                          scale=rstd[h][:, u:u + 1])
                last.then_inc(n_x1, 1)

            def p_copy(s, h, i):
                act.wait_ge(n_p, after(s))
                act.wait_ge(p_out[h], i * 16)
                act.activation(p_sb[h][:, :, :], banks(2, 4)[:, 0:TS * DH].rearrange("p (t f) -> p t f", f=DH), ACT.Copy)\
                   .then_inc(n_pc, 1)

            def exps(s, h, i):
                act.wait_ge(t_logits, after(s))
                for u in range(TS):
                    last = act.activation(sm[h][:, u, :], sm[h][:, u, :], ACT.Exp, bias=negmax[h][:, u:u + 1],
                                          accum_out=esum[h][:, u:u + 1])
                last.then_inc(t_exp, 1)

            def std_of(made, done, mv_h, std_h, s):
                act.wait_ge(made, after(s))
                act.activation(std_h[:, :], mv_h[:, :, 1], ACT.Sqrt, bias=eps[:, :]).then_inc(done, 1)

            def std_x(s, h, i):
                std_of(v_var, v_std, mv[h], std[h], s)
            node_steps(act, 3, (2, normed), (0, exps), (3, p_copy), (1, std_x))

            def put_b2(j):
                return act.activation(banks(4 + j % 2).rearrange("p (k f) -> p k f", k=K),
                                      b2_sb[:, :].unsqueeze(1).to_broadcast([P, K, D]), ACT.Copy)

            act.wait_ge(c_open, 1)
            for j in range(2):
                put_b2(j).then_inc(c_b2, 1)

            def hidden(g, j, it):
                act.wait_ge(c_t, after(g))
                act.wait_ge(c_m, after(g - 2))
                act.activation(hid[j % 2][:, :, :].rearrange("p c e -> p (c e)"), banks(2, 2), ACT.Relu).then_inc(c_hid, 1)

            def parts(g, j, it):
                act.wait_ge(c_m, after(g))
                act.wait_ge(c_sum, after(g - 2))
                act.activation(msg[j % 2][:, 0, :, :].rearrange("p k f -> p (k f)"), banks(4 + j % 2), ACT.Relu)\
                   .then_inc(c_part, 1)
                act.wait_ge(c_rest, after(g))
                act.activation(msg[j % 2][:, 1, :, :], rest[j % 2][:, :, :], ACT.Copy).then_inc(c_part2, 1)
                put_b2(j).then_inc(c_b2, 1)
            stage_order(act, 3, ((3, parts), (1, hidden)))

            def normed_f(s, h, base, shift_h, rstd_h, into):
                for u in range(TS):
                    last = act.activation(into[:, u, :], banks(base, 2)[:, u * D:(u + 1) * D], ACT.Identity,
                                          bias=shift_h[:, u:u + 1], scale=rstd_h[:, u:u + 1])
                return last

            def norm_1(s, h, i):
                act.wait_ge(f_shift, after(s))
                act.wait_ge(f_t, after(s - 2))
                normed_f(s, h, 6 * h, shift[h], rstd[h], row[h]).then_inc(f_nrm, 1)

            def norm_2(s, h, i):
                act.wait_ge(f_shift2, after(s))
                act.wait_ge(f_out[h], i * 16)
                normed_f(s, h, 4, shift2[h], rstd2[h], sm[h]).then_inc(f_o, 1)

            def relu_f(s, h, i):
                act.wait_ge(f_t, after(s))
                act.wait_ge(f_lin, after(s - 2))
                act.activation(row_t[h][:, :], banks(2, 2)[:, 0:TS * P], ACT.Relu, bias=beta_sb[:, :], scale=gamma_sb[:, :])\
                   .then_inc(f_z, 1)

            def std_1(s, h, i):
                std_of(f_var, f_std, mv[h], std[h], s)

            def std_2(s, h, i):
                std_of(f_var2, f_std2, mv2[h], std2[h], s)
            node_steps(act, 1, (1, relu_f), (0, std_1), (0, norm_1), (1, std_2), (1, norm_2))

        @block.tensor
        def _(pe):
            credit(pe, a_sum, m_mul, b_mix, b_sum, n_t, n_p, c_edge, c_t, c_m, c_sum, f_res, f_t, f_lin)
            pe.wait_ge(cst, 1)

            def window_sums(rows_j, hots, hots_b, bank):
                for k in range(K):
                    pe.matmul(ps[:, bank, 0:W], rows_j[:, k, :], hots[:, k, :], start=(k == 0), stop=(k == K - 1))
                for k in range(K):
                    last = pe.matmul(ps[:, bank, W:2 * W], ones_b[:, :], hots_b[:, k, :], start=(k == 0), stop=(k == K - 1))
                return last

            pe.wait_ge(meta_in, 32)
            count = counter(pe, "x_pe")

            def sums_a(g, j, it):
                lo, wins = group_meta(pe, g)
                pe.wait_ge(a_got[j], it * (16 * K) + 16 * K)

                def further(w, n):
                    pe.wait_ge(ax_hot, n + 1)
                    window_sums(rows_a[j], hot_x, hot_xb, 2).then_inc(ax_sum, 1)
                further_windows(pe, count, wins, further)
                pe.wait_ge(a_hot, after(g))
                pe.wait_ge(a_added, after(g - 2))
                window_sums(rows_a[j], hot[j], hot_b[j], j % 2).then_inc(a_sum, 1)
            groups(pe, sums_a)

            pe.wait_ge(ld_w, 16 * LOADS_W)

            def mul_m(n, h, i):
                pe.wait_ge(m_picked, after(n))
                pe.wait_ge(m_made, after(n - 2))
                for t in range(MT):
                    last = pe.matmul(banks(2 * h, 2)[:, t * D:(t + 1) * D], sum_t[h][:, t, :], W0_sb[:, :],
                                     start=True, stop=True)
                last.then_inc(m_mul, 1)
            stage_order(pe, 0, ((0, mul_m),), NB, 2, 1)
            pe.wait_ge(m_made, after(NB - 1))

            def mixes(hots, same_j, bank):
                for k in range(K):
                    last = pe.matmul(ps[0:W, bank, k * P:(k + 1) * P], hots[:, k, :], same_j[:, k, :], start=True, stop=True)
                return last

            def sums_of(mix_j, win, base, stop):
                for k in range(K):
                    c = (k % 2) * DX
                    last = pe.matmul(ps[:, base + k // 2, c:c + DX], mix_j[:, k, :], win[:, :], start=False,
                                     stop=stop, skip_group_check=True)
                return last

            pe.reg_mov(count, 0)

            def sums_b(g, j, it):
                lo, wins = group_meta(pe, g)
                base = 2 + 2 * (j % 2)
                pe.wait_ge(b_same, after(g))
                pe.wait_ge(b_mixed, after(g - 2))
                mixes(hot_b[j], same[j], j % 2).then_inc(b_mix, 1)
                pe.wait_ge(b_sums, after(g - 2))
                for b in range(2):
                    pe.matmul(ps[:, base + b, 0:2 * DX], zeros_b[0:1, 0:P], zeros_b[0:1, 0:2 * DX], start=True,
                              stop=False, skip_group_check=True)

                def further(w, n):
                    pe.wait_ge(bx_hot, n + 1)
                    mixes(hot_xb, same[j], 6).then_inc(bx_mix, 1)
                    pe.wait_ge(bx_mixed, n + 1)
                    pe.wait_ge(bx_win, (n + 1) * 16)
                    sums_of(mix_x, m_win_x, base, False).then_inc(bx_sum, 1)
                further_windows(pe, count, wins, further)
                pe.wait_ge(b_mixed, after(g))
                pe.wait_ge(b_win_in[j], it * 16 + 16)
                sums_of(mix[j], m_win[j], base, True).then_inc(b_sum, 1)
            groups(pe, sums_b)

            def p_tiles(s, h, i):
                pe.wait_ge(n_x1, after(s))
                pe.wait_ge(n_tc, after(s - 1))
                for u in range(TS):
                    last = pe.transpose(banks(0, 2)[:, u * P:(u + 1) * P], row[h][:, u, :], ident[:, :])
                last.then_inc(n_t, 1)
                pe.wait_ge(n_tc, after(s))
                pe.wait_ge(n_pc, after(s - 1))
                for u in range(TS):
                    to_u = banks(2, 4)[:, u * DH:(u + 1) * DH]
                    pe.matmul(to_u, ones_b[0:3, :], bias3[:, D:], start=True, stop=False)
                    last = pe.matmul(to_u, row_t[0][:, u * P:(u + 1) * P], W1a_sb[:, :], start=False, stop=True)
                last.then_inc(n_p, 1)
            node_steps(pe, 0, (0, p_tiles))

            pe.wait_ge(n_pc, after(STEPS - 1))
            for b in range(2):
                last = pe.matmul(banks(4 + b), zeros_b[0:1, 0:P], zeros_b[0:1, :], start=True, stop=True)
            last.then_inc(c_open, 1)

            def edge_part(g, j, it):
                pe.wait_ge(ea_in[j], it * 16 + 16)
                pe.wait_ge(c_pre, after(g - 1))
                for k in range(K // 2):
                    for half in range(2):
                        rows_of_half = slice(half * DE, (half + 1) * DE)
                        last = pe.matmul(banks(half)[:, k * DH:(k + 1) * DH], ea[j][rows_of_half, k * P:(k + 1) * P],
                                         W1b_sb[rows_of_half, :], start=True, stop=True)
                last.then_inc(c_edge, 1)

            def transposes(g, j, it):
                pe.wait_ge(c_pre, after(g))
                pe.wait_ge(c_hid, after(g - 1))
                for k in range(K):
                    for c in range(2):
                        last = pe.transpose(banks(2 + c)[:, k * P:(k + 1) * P], pre[j % 2][:, k, c * P:(c + 1) * P], ident[:, :])
                last.then_inc(c_t, 1)

            def message(g, j, it):
                bank = banks(4 + j % 2)
                pe.wait_ge(c_hid, after(g))
                pe.wait_ge(c_b2, after(g))
                for k in range(K):
                    for c in range(2):
                        last = pe.matmul(bank[:, k * P:(k + 1) * P], hid[j % 2][:, c, k * P:(k + 1) * P], W2_sb[:, c, :],
                                         start=False, stop=(c == 1), skip_group_check=True)
                last.then_inc(c_m, 1)

            def message_sums(j, hots, to_window):
                for k in range(K):
                    for q in range(3):
                        last = pe.matmul(to_window, msg[j % 2][:, q, k, :], hots[:, k, :], start=(k == 0 and q == 0),
                                         stop=(k == K - 1 and q == 2))
                return last

            pe.reg_mov(count, 0)

            def sums_c(g, j, it):
                lo, wins = group_meta(pe, g)
                pe.wait_ge(c_msg, after(g))

                def further(w, n):
                    pe.wait_ge(cx_hot, n + 1)
                    message_sums(j, hot_xb, ps[:, 7, 0:W]).then_inc(cx_sum, 1)
                further_windows(pe, count, wins, further)
                pe.wait_ge(c_hot, after(g))
                pe.wait_ge(c_added, after(g - 1))
                message_sums(j, hot_b[j], ps[:, 6, 0:W]).then_inc(c_sum, 1)
            stage_order(pe, 3, ((0, edge_part), (1, transposes), (2, message), (3, sums_c)))

            def add_x1(base, s):
                flat = x1[:, :, :].rearrange("p t f -> p (t f)")
                pe.matmul(banks(base), ident[:, :], flat[:, bass.ds(s * (TS * D), 4 * D)], start=True, stop=False,
                          skip_group_check=True)
                return pe.matmul(banks(base + 1)[:, 0:3 * D], ident[:, :], flat[:, bass.ds(s * (TS * D) + 4 * D, 3 * D)],
                                 start=True, stop=False, skip_group_check=True)

            def residual_f(s, h, i):
                pe.wait_ge(f_agg, after(s))
                pe.wait_ge(f_nrm, after(s - 2))
                add_x1(6 * h, s)
                for u in range(TS):
                    last = pe.matmul(banks(6 * h, 2)[:, u * D:(u + 1) * D], agg_t[h][:, u, :], ident[:, :],
                                     start=False, stop=True, skip_group_check=True)
                last.then_inc(f_res, 1)

            def linear_f(s, h, i):
                pe.wait_ge(f_o, after(s - 1))
                add_x1(4, s)
                bu_k = bias3_k[:, :, :].rearrange("q k f -> q (k f)")
                for b, n in ((0, 4 * D), (1, 3 * D)):
                    pe.matmul(banks(4 + b)[:, 0:n], ones_b[0:3, :], bu_k[:, 0:n], start=False, stop=False,
                              skip_group_check=True)
                pe.wait_ge(f_z, after(s))
                for u in range(TS):
                    last = pe.matmul(banks(4, 2)[:, u * D:(u + 1) * D], row_t[h][:, u * P:(u + 1) * P], Wu_sb[:, :],
                                     start=False, stop=True, skip_group_check=True)
                last.then_inc(f_lin, 1)

            def transposes_f(s, h, i):
                pe.wait_ge(f_nrm, after(s))
                pe.wait_ge(f_z, after(s - 1))
                for u in range(TS):
                    last = pe.transpose(banks(2, 2)[:, u * P:(u + 1) * P], row[h][:, u, :], ident[:, :])
                last.then_inc(f_t, 1)
            pe.wait_ge(c_b2, after(NG + 1))
            for h in range(2):
                pe.wait_ge(x1_kept[h], 16 * ((STEPS + 1 - h) // 2))
            node_steps(pe, 1, (1, transposes_f), (0, residual_f), (1, linear_f))

        @block.vector
        def _(dve):
            credit(dve, a_hot, a_added, b_same, b_to, t_logits, n_tc, c_pre, c_rest, c_msg, c_hot, c_added,
                   m_made, t_inv, v_var, v_shift, f_var, f_shift, f_var2, f_shift2)
            dve.wait_ge(ld_dst_g, 16)
            dve.tensor_reduce(lohi[:, 0, :], dst_g[:, :, :], AX.X, ALU.min)
            dve.tensor_reduce(lohi[:, 1, :], dst_g[:, :, :], AX.X, ALU.max)
            dve.drain()
            dve.tensor_tensor(span_i[:, :], lohi[:, 1, :], lohi[:, 0, :], ALU.subtract)
            dve.drain()
            dve.tensor_scalar(span_i[:, :], span_i[:, :], W.bit_length() - 1, None, ALU.arith_shift_right)
            dve.drain()
            dve.tensor_scalar(wins[:, :], span_i[:, :], 1.0, None, ALU.add)
            dve.drain()
            dve.scalar_tensor_tensor(meta_i[:, :], lohi[:, 0, :], float(P), wins[:, :], ALU.mult, ALU.add)
            dve.drain().then_inc(meta_made, 2)
            dve.memset(acc[:, 0, :], 0.0)
            dve.wait_ge(cst, 1)
            dve.tensor_copy(iota[:, :], iota_i[:, :])
            dve.tensor_copy(spare[:, :], spare_i[:, :])
            dve.tensor_copy(win_start[:, :], win_start_i[:, :])
            dve.wait_ge(ld_dst, 16)
            dve.wait_ge(meta_in, 32)
            dve.tensor_tensor(rel[:, :, :], dst_i[:, :, :], lo_bc[:, :].unsqueeze(2).to_broadcast([P, NG, K]), ALU.subtract)
            dve.drain()

            iota_k = iota[:, :].unsqueeze(1).to_broadcast([P, K, W])

            def rel_of(g):
                return rel[:, bass.ds(g, 1), :].rearrange("p o k -> p (o k)")

            def one_hot(hots, places):
                return dve.tensor_tensor(hots[:, :, :], iota_k, places.unsqueeze(2).to_broadcast([P, K, W]), ALU.is_equal)

            def further_place(g, w):
                dve.tensor_scalar(rel_x[:, :], rel_of(g), win_start[:, bass.ds(w, 1)], None, ALU.subtract)
                dve.drain()

            count = counter(dve, "x_dve")

            dve.wait_ge(counts_zero, 1)

            def hot_a(g, j, it):
                dve.wait_ge(a_sum, after(g - RING))
                one_hot(hot[j], rel_of(g))
                one_hot(hot_b[j], rel_of(g)).then_inc(a_hot, 1)

            def sums_a(g, j, it):
                lo, wins_g = group_meta(dve, g)

                def further(w, n):
                    further_place(g, w)
                    one_hot(hot_x, rel_x[:, :])
                    one_hot(hot_xb, rel_x[:, :]).then_inc(ax_hot, 1)
                    dve.wait_ge(ax_sum, n + 1)
                    at = acc[:, :, bass.ds(window_at(lo, w), W)]
                    dve.tensor_tensor(at, at, ps[:, 2, 0:2 * W].rearrange("p (a w) -> p a w", a=2), ALU.add)
                    dve.drain()
                further_windows(dve, count, wins_g, further)
                dve.wait_ge(a_sum, after(g))
                dve.wait_ge(a_added, after(g - 1))
                at = acc[:, :, bass.ds(lo, W)]
                dve.tensor_tensor(at, at, ps[:, j % 2, 0:2 * W].rearrange("p (a w) -> p a w", a=2), ALU.add)\
                   .then_inc(a_added, 1)
            stage_order(dve, 1, ((0, hot_a), (1, sums_a)))

            dve.wait_ge(ld_src, 16)
            dve.tensor_copy(src_f[:, :, :], src_i[:, :, :])

            dve.wait_ge(ld_w, 16 * LOADS_W)
            for q in range(3):
                dve.tensor_copy(bias_b[:, :], bias[:, :])
                dve.drain()
                if q == 0:
                    dve.tensor_scalar(bias3[:, :], bias_b[:, :], ident[0:3, 0:1], None, ALU.mult)
                else:
                    dve.scalar_tensor_tensor(bias3[:, :], bias_b[:, :], ident[0:3, q:q + 1], bias3[:, :],
                                             ALU.mult, ALU.add)
                dve.tensor_tensor(bias[:, :], bias[:, :], bias_b[:, :], ALU.subtract)
                dve.drain()
            dve.tensor_copy(bias3_k[:, :, :], bias3[:, 0:D].unsqueeze(1).to_broadcast([3, K, D]))

            dve.wait_ge(m_counts, 16)
            dve.tensor_scalar(inv_deg[:, :], inv_deg[:, :], 1.0, None, ALU.max)
            dve.drain()
            dve.reciprocal(inv_deg[:, :], inv_deg[:, :])
            dve.drain()

            def scale_m(n, h, i):
                dve.wait_ge(m_mul, after(n))
                dve.tensor_tensor(m_sb[:, bass.ds(n * MT, MT), 0:D], banks(2 * h, 2)[:, 0:MT * D].rearrange("p (t f) -> p t f", f=D),
                                  inv_deg[:, bass.ds(n * MT, MT)].unsqueeze(2).to_broadcast([P, MT, D]), ALU.mult)\
                   .then_inc(m_made, 1)
            stage_order(dve, 0, ((0, scale_m),), NB, 2, 1)

            dve.reg_mov(count, 0)

            def compare_b(g, j, it):
                lo, wins_g = group_meta(dve, g)
                srcs = src_f[:, bass.ds(g, 1), :].rearrange("p o k -> p (o k)")
                dve.wait_ge(b_src_in[j], it * 16 + 16)
                dve.wait_ge(b_sum, after(g - RING))
                one_hot(hot_b[j], rel_of(g))
                dve.tensor_tensor(same[j][:, :, :], src_b[j][:, :, :], srcs.unsqueeze(2).to_broadcast([P, K, P]), ALU.is_equal)\
                   .then_inc(b_same, 1)
                dve.drain()
                dve.tensor_tensor(same_before[:, :, :], same[j][:, :, :], earlier[:, :].unsqueeze(1).to_broadcast([P, K, P]), ALU.mult)
                dve.drain()
                dve.tensor_reduce(dup[:, :], same_before[:, :, :], AX.X, ALU.add)
                dve.drain()
                dve.tensor_scalar(spare_if[:, :], dup[:, :], 0.0, spare[:, 0:1], ALU.is_gt, ALU.mult)
                dve.drain()
                for k in range(K):
                    dve.wait_ge(b_put[j][k], it * 16)
                dve.tensor_tensor(to[j][:, :], spare_if[:, :], srcs, ALU.max).then_inc(b_to, 1)

                def further(w, n):
                    dve.wait_ge(bx_sum, n)
                    further_place(g, w)
                    one_hot(hot_xb, rel_x[:, :]).then_inc(bx_hot, 1)
                    dve.wait_ge(bx_hot, n + 1)
                further_windows(dve, count, wins_g, further)
            groups(dve, compare_b)

            def inv_sum(s, h, i):
                dve.wait_ge(t_exp, after(s))
                dve.reciprocal(esum[h][:, :], esum[h][:, :]).then_inc(t_inv, 1)

            def logits(s, h, i):
                dve.wait_ge(t_half, after(s))
                dve.wait_ge(t_y, after(s - 2))
                dve.tensor_tensor(tab[h][:, 0, :], tab[h][:, 0, :], tab[h][:, 2, :], ALU.add)
                dve.drain()
                t = tab[h][:, 0, :].rearrange("p (t f) -> p t f", f=DX)
                dve.tensor_scalar(inv[h][:, :], t[:, :, D:DX].rearrange("p t o -> p (t o)"), 1.0, None, ALU.max)
                dve.drain()
                dve.reciprocal(inv[h][:, :], inv[h][:, :])
                dve.drain()
                for u in range(TS):
                    dve.scalar_tensor_tensor(sm[h][:, u, :], t[:, u, 0:D], inv[h][:, u:u + 1], b0_sb[:, :], ALU.mult, ALU.add)
                dve.drain()
                dve.tensor_reduce(negmax[h][:, :], sm[h][:, :, :], AX.X, ALU.max)
                dve.drain()
                dve.tensor_scalar(negmax[h][:, :], negmax[h][:, :], -1.0, None, ALU.mult).then_inc(t_logits, 1)

            def moments(rows_of, into):
                for u in range(TS):
                    dve.bn_stats(stats[:, u, :], rows_of(u))
                dve.drain()
                for u in range(TS):
                    last = dve.bn_aggr(into[:, u, :], stats[:, u, :])
                return last

            def stats_x(s, h, i):
                dve.wait_ge(t_y, after(s))
                moments(lambda u: y[h][:, u, :], mv[h]).then_inc(v_var, 1)
                dve.drain()

            def copy_t(s, h, i):
                dve.wait_ge(n_t, after(s))
                dve.wait_ge(n_p, after(s - 1))
                dve.tensor_copy(row_t[0][:, :], banks(0, 2)[:, 0:TS * P]).then_inc(n_tc, 1)

            def shift_x(s, h, i):
                dve.wait_ge(v_std, after(s))
                dve.reciprocal(rstd[h][:, :], std[h][:, :])
                dve.drain()
                dve.scalar_tensor_tensor(shift[h][:, :], mv[h][:, :, 0], -1.0, rstd[h][:, :], ALU.mult, ALU.mult)\
                   .then_inc(v_shift, 1)
            node_steps(dve, 3, (3, copy_t), (1, inv_sum), (2, shift_x), (0, logits), (1, stats_x))

            dve.wait_ge(acc_zero, 1)
            dve.reg_mov(count, 0)

            def rest_c(g, j, it):
                dve.wait_ge(c_part, after(g))
                dve.wait_ge(c_part2, after(g - 2))
                dve.wait_ge(c_msg, after(g - 2))
                dve.scalar_tensor_tensor(rest[j % 2][:, :, :].rearrange("p k f -> p (k f)"), banks(4 + j % 2), 0.0,
                                         msg[j % 2][:, 0, :, :].rearrange("p k f -> p (k f)"), ALU.max, ALU.subtract)\
                   .then_inc(c_rest, 1)

            def add_p(g, j, it):
                dve.wait_ge(c_got[j], it * (16 * K) + 16 * K)
                dve.wait_ge(c_t, after(g - 2))
                dve.wait_ge(c_edge, after(g))
                dve.tensor_tensor(pre[j % 2][:, :, :].rearrange("p k f -> p (k f)"), banks(0, 2),
                                  rows[j][:, :, :].rearrange("p k f -> p (k f)"), ALU.add).then_inc(c_pre, 1)

            def third_part(g, j, it):
                dve.wait_ge(c_part2, after(g))
                dve.tensor_tensor(msg[j % 2][:, 2, :, :], rest[j % 2][:, :, :], msg[j % 2][:, 1, :, :], ALU.subtract)\
                   .then_inc(c_msg, 1)

            def hot_c(g, j, it):
                dve.wait_ge(c_sum, after(g - RING))
                one_hot(hot_b[j], rel_of(g)).then_inc(c_hot, 1)

            def sums_c(g, j, it):
                lo, wins_g = group_meta(dve, g)

                def further(w, n):
                    further_place(g, w)
                    one_hot(hot_xb, rel_x[:, :]).then_inc(cx_hot, 1)
                    dve.wait_ge(cx_sum, n + 1)
                    at = acc[:, 0, bass.ds(window_at(lo, w), W)]
                    dve.tensor_tensor(at, at, ps[:, 7, 0:W], ALU.add)
                    dve.drain()
                further_windows(dve, count, wins_g, further)
                dve.wait_ge(c_sum, after(g))
                dve.wait_ge(c_added, after(g - 1))
                at = acc[:, 0, bass.ds(lo, W)]
                dve.tensor_tensor(at, at, ps[:, 6, 0:W], ALU.add).then_inc(c_added, 1)
            stage_order(dve, 4, ((3, rest_c), (4, sums_c), (0, add_p), (3, third_part), (0, hot_c)))

            def stats_1(s, h, i):
                dve.wait_ge(f_res, after(s))
                moments(lambda u: banks(6 * h, 2)[:, u * D:(u + 1) * D], mv[h]).then_inc(f_var, 1)
                dve.drain()

            def stats_2(s, h, i):
                dve.wait_ge(f_lin, after(s))
                moments(lambda u: banks(4, 2)[:, u * D:(u + 1) * D], mv2[h]).then_inc(f_var2, 1)
                dve.drain()

            def shift_1(s, h, i):
                dve.wait_ge(f_std, after(s))
                dve.reciprocal(rstd[h][:, :], std[h][:, :])
                dve.drain()
                dve.scalar_tensor_tensor(shift[h][:, :], mv[h][:, :, 0], -1.0, rstd[h][:, :], ALU.mult, ALU.mult)\
                   .then_inc(f_shift, 1)

            def shift_2(s, h, i):
                dve.wait_ge(f_std2, after(s))
                dve.reciprocal(rstd2[h][:, :], std2[h][:, :])
                dve.drain()
                dve.scalar_tensor_tensor(shift2[h][:, :], mv2[h][:, :, 0], -1.0, rstd2[h][:, :], ALU.mult, ALU.mult)\
                   .then_inc(f_shift2, 1)
            node_steps(dve, 1, (0, stats_1), (0, shift_1), (1, stats_2), (1, shift_2))


_INS = ["x", "src_cols", "src_all", "dst_all", "dst_groups", "src_row", "edge_t", "L0_gnn_W", "L0_gnn_b", "L1_gnn_W1", "L1_gnn_b1",
        "L1_gnn_W2", "L1_gnn_b2", "L1_gnn_gamma", "L1_gnn_beta", "L1_gnn_Wu", "L1_gnn_bu"]


def kernel(**inputs):
    import numpy as np
    import concourse.bacc as bacc
    from concourse.bass_utils import run_bass_kernel_spmd

    a = {k: np.asarray(v) for k, v in inputs.items()}
    x = np.zeros((NPAD, D), a["x"].dtype)
    x[:NODES] = a["x"]
    src = np.full(EPAD, NODES, np.int32)
    dst = np.full(EPAD, NODES, np.int32)
    src[:EDGES] = a["src"]
    dst[:EDGES] = a["dst"]
    edge_t = np.zeros((DE, EPAD), a["edge_attr_64"].dtype)
    edge_t[:, :EDGES] = a["edge_attr_64"].T
    edge_t = edge_t.reshape(DE, NG, 2, GE // 2).transpose(2, 0, 1, 3).reshape(2 * DE, NG * (GE // 2))
    a.update(x=x, edge_t=edge_t, src_row=src.reshape(NG, GE), dst_groups=dst.reshape(NG // 2, 2, GE),
             src_cols=src.reshape(NG, K, P).transpose(0, 2, 1), src_all=src.reshape(NG, K, P).transpose(2, 0, 1),
             dst_all=dst.reshape(NG, K, P).transpose(2, 0, 1))

    nc = bacc.Bacc("TRN2", target_bir_lowering=False, num_devices=1)
    arrays, args = {}, []
    for name in _INS:
        arrays[f"in_{name}"] = np.ascontiguousarray(a[name])
        args.append(nc.dram_tensor(f"in_{name}", arrays[f"in_{name}"].shape, mybir.dt.from_np(a[name].dtype),
                                   kind="ExternalInput").ap())
    args.append(nc.dram_tensor("out_rows", (NPAD, D), F32, kind="ExternalOutput").ap())
    build(nc, *args)
    r = run_bass_kernel_spmd(nc, [arrays], core_ids=[0])
    return r.results[0]["out_rows"][:NODES]
```
